# Optimizing a Trainium2 kernel written in Bass

```python
import numpy as np
import jax
import jax.numpy as jnp

def _softmax(x, axis=-1):
    return jax.nn.softmax(x, axis=axis)

def _gelu(x):
    return jax.nn.gelu(x, approximate=True)

def _silu(x):
    return jax.nn.silu(x)

def _sigmoid(x):
    return jax.nn.sigmoid(x)

def _layernorm(x, axis=-1, eps=1e-05):
    m = jnp.mean(x, axis=axis, keepdims=True)
    v = jnp.var(x, axis=axis, keepdims=True)
    return (x - m) / jnp.sqrt(v + eps)

def _scatter_add(tgt, idx, src, axis=0):
    return tgt.at[idx].add(src)

def _segment_sum(src, seg, n):
    return jax.ops.segment_sum(src, seg, n)
kernel_name = 'mk_adaln_ffn_d1_seqx_r2_4e7306'

def setup_inputs(seed: int=0):
    np.random.seed(seed)
    _w = jnp.asarray

    def _rec_inputs():
        import jax
        import jax.numpy as jnp
        _rk = jax.random.key(seed)
        x = -8.015e-05 + 0.9999 * jax.random.normal(jax.random.fold_in(_rk, 1), (16, 512, 1024), jnp.float32)
        _lenS = 512 - jax.random.randint(jax.random.fold_in(_rk, 7), (16,), 0, max(1, 512 // 4) + 1, jnp.int32)
        _lenS2 = 512 - jax.random.randint(jax.random.fold_in(_rk, 8), (16,), 0, max(1, 512 // 4) + 1, jnp.int32)
        cond_1024 = 0.00191187 + 0.999416 * jax.random.normal(jax.random.fold_in(_rk, 11), (16, 512), jnp.float32)
        return (x, cond_1024)
    x, cond_1024 = _rec_inputs()

    def _L0_cond_setup():
        import jax, jax.numpy as jnp
        import numpy as np
        B, N, V_DIM, Q_DIM = (128, 100, 1024, 512)
        key = jax.random.key(seed)
        k1, k2, k3, k4 = jax.random.split(key, 4)
        v = jax.random.normal(k1, (B, N, V_DIM), dtype=jnp.float32)
        q = jax.random.normal(k2, (B, Q_DIM), dtype=jnp.float32)
        W3 = jax.random.normal(k3, (Q_DIM, V_DIM), dtype=jnp.float32) * (1.0 / np.sqrt(Q_DIM))
        b3 = jnp.zeros((V_DIM,), dtype=jnp.float32)
        W2 = jax.random.normal(k4, (V_DIM, V_DIM), dtype=jnp.float32) * (1.0 / np.sqrt(V_DIM))
        b2 = jnp.zeros((V_DIM,), dtype=jnp.float32)
        return {'v': v, 'q': q, 'W3': W3, 'b3': b3, 'W2': W2, 'b2': b2}
    _L0_cond_all = _L0_cond_setup()
    _L0_cond_in = {k: v for k, v in _L0_cond_all.items() if k in ('W3', 'b3', 'W2', 'b2')}
    del _L0_cond_all

    def _L0_ffn_setup():
        import jax, jax.numpy as jnp
        import numpy as np
        B, S, D, E, R, TOP_K = (4, 2048, 1024, 6, 16, 2)
        key = jax.random.key(seed)
        ks = jax.random.split(key, 9)
        scale = 0.02
        return {'x': jax.random.normal(ks[0], (B, S, D), dtype=jnp.float32), 'W_base': jax.random.normal(ks[1], (D, D), dtype=jnp.float32) * scale, 'b_base': jax.random.normal(ks[2], (D,), dtype=jnp.float32) * scale, 'A_s': jax.random.normal(ks[3], (D, R), dtype=jnp.float32) * scale, 'B_s': jax.random.normal(ks[4], (R, D), dtype=jnp.float32) * scale, 'A_r': jax.random.normal(ks[5], (E, D, R), dtype=jnp.float32) * scale, 'B_r': jax.random.normal(ks[6], (E, R, D), dtype=jnp.float32) * scale, 'W_router': jax.random.normal(ks[7], (D, E), dtype=jnp.float32) * scale, 'b_router': jax.random.normal(ks[8], (E,), dtype=jnp.float32) * scale}
    _L0_ffn_all = _L0_ffn_setup()
    _L0_ffn_in = {k: v for k, v in _L0_ffn_all.items() if k in ('W_base', 'b_base', 'A_s', 'B_s', 'A_r', 'B_r', 'W_router', 'b_router')}
    del _L0_ffn_all
    return {'x': x, 'cond_1024': cond_1024, 'L0_cond_W3': _L0_cond_in['W3'], 'L0_cond_b3': _L0_cond_in['b3'], 'L0_cond_W2': _L0_cond_in['W2'], 'L0_cond_b2': _L0_cond_in['b2'], 'L0_ffn_W_base': _L0_ffn_in['W_base'], 'L0_ffn_b_base': _L0_ffn_in['b_base'], 'L0_ffn_A_s': _L0_ffn_in['A_s'], 'L0_ffn_B_s': _L0_ffn_in['B_s'], 'L0_ffn_A_r': _L0_ffn_in['A_r'], 'L0_ffn_B_r': _L0_ffn_in['B_r'], 'L0_ffn_W_router': _L0_ffn_in['W_router'], 'L0_ffn_b_router': _L0_ffn_in['b_router']}

def reference(x, cond_1024, L0_cond_W3, L0_cond_b3, L0_cond_W2, L0_cond_b2, L0_ffn_W_base, L0_ffn_b_base, L0_ffn_A_s, L0_ffn_B_s, L0_ffn_A_r, L0_ffn_B_r, L0_ffn_W_router, L0_ffn_b_router):
    import jax
    import jax.numpy as jnp

    def _L0_cond_ref(v, q, W3, b3, W2, b2):
        import jax, jax.numpy as jnp
        import numpy as np
        B, N, V_DIM, Q_DIM = (128, 100, 1024, 512)
        q_emb = jax.nn.relu(q @ W3 + b3)
        n = v.shape[1]
        v_sum = jnp.sum(v, axis=1, keepdims=True)
        x = (n * v + v_sum) * q_emb[:, None, :]
        return jax.nn.relu(x @ W2 + b2)

    def _L0_ffn_ref(x, W_base, b_base, A_s, B_s, A_r, B_r, W_router, b_router):
        import jax, jax.numpy as jnp
        import numpy as np
        B, S, D, E, R, TOP_K = (4, 2048, 1024, 6, 16, 2)
        base_out = jax.lax.stop_gradient(jnp.einsum('bsd,df->bsf', x, W_base) + b_base)
        shared_out = jnp.einsum('bsr,rf->bsf', jnp.einsum('bsd,dr->bsr', x, A_s), B_s)
        gates = jax.nn.softmax(jnp.einsum('bsd,de->bse', x, W_router) + b_router, axis=-1)
        topk_w, topk_i = jax.lax.top_k(gates, TOP_K)
        w_per_e = jnp.sum(topk_w[..., None] * jax.nn.one_hot(topk_i, E, dtype=x.dtype), axis=2)
        h = jnp.einsum('bsd,edr->bser', x, A_r)
        hw = h * w_per_e[..., None]
        routed_out = jnp.einsum('bser,erf->bsf', hw, B_r)
        return base_out + shared_out + routed_out
    x = x + _L0_ffn_ref(_L0_cond_ref(x, cond_1024, L0_cond_W3, L0_cond_b3, L0_cond_W2, L0_cond_b2), L0_ffn_W_base, L0_ffn_b_base, L0_ffn_A_s, L0_ffn_B_s, L0_ffn_A_r, L0_ffn_B_r, L0_ffn_W_router, L0_ffn_b_router)
    return x

_drawn_inputs = setup_inputs


def setup_inputs(seed=0):
    import zlib

    import numpy as np

    out = dict(_drawn_inputs(seed))
    spreads = {'L0_cond_b3': (0.0, 0.1), 'L0_cond_b2': (0.0, 2.0)}
    factors = {'L0_ffn_b_base': 200.0, 'L0_ffn_b_router': 200.0}
    for name, (base, spread) in spreads.items():
        noise = np.random.default_rng([zlib.crc32(name.encode()), seed]).standard_normal(out[name].shape)
        drawn = base * np.exp(spread * noise) if base else spread * noise
        out[name] = jnp.asarray(drawn.astype(out[name].dtype))
    for name, factor in factors.items():
        out[name] = (out[name] * factor).astype(out[name].dtype)
    return out
```

```python
from contextlib import ExitStack

import concourse.bass as bass
from concourse import mybir

F32 = mybir.dt.float32
F32R = mybir.dt.float32r
ALU = mybir.AluOpType
ACT = mybir.ActivationFunctionType
AX = mybir.AxisListType

P = 128
PAIR = 2


def adaln_ffn(nc, xT, condT, w3, b3, w2, b2, wbase, bbase, acat, bcat, brouter, outT, E, R):
    NB, K, _, T = xT.shape
    D = K * P
    G = K // PAIR
    GW = PAIR * P
    QK = condT.shape[1]
    AC = E + (E + 1) * R
    TT = T // P
    NCH = wbase.shape[0]
    CW = wbase.shape[2]
    YS = 4
    HALF = K // 2
    FIRST = 4
    FK = K // FIRST
    WARM = 8
    EARLY_W = 2

    y_dram = nc.dram_tensor("y_scratch", (NB, K, P, T), F32, kind="Internal").ap()

    with ExitStack() as ctx:
        def sb(name, shape, dt=F32, stack=ctx):
            return stack.enter_context(nc.sbuf_tensor(name, shape, dt))

        def sem(name):
            return ctx.enter_context(nc.semaphore(name))

        act_hi = sb("act_hi", [P, K, T], F32R)
        act_lo = sb("act_lo", [P, K, T], F32R)
        stage = sb("stage", [P, K, T])
        yring = sb("yring", [P, YS, T])
        a_hi = sb("a_hi", [P, K, AC], F32R)
        a_lo = sb("a_lo", [P, K, AC], F32R)
        low_hi = sb("low_hi", [AC, D], F32R)
        low_lo = sb("low_lo", [AC, D], F32R)
        wstage = sb("wstage", [P, D])
        cond_sb = sb("cond_sb", [P, QK, NB])
        b3_sb = sb("b3_sb", [P, K])
        b2_sb = sb("b2_sb", [P, K])
        bb_sb = sb("bb_sb", [P, K])
        br_sb = sb("br_sb", [P, E])
        qn = sb("qn", [P, K, NB])
        vsum = sb("vsum", [P, K])
        vmean = sb("vmean", [P, K])
        ident = sb("ident", [P, P])
        earlier = sb("earlier", [P, E, E])
        wrow = sb("wrow", [P, TT, AC])

        early = ExitStack()
        w3_raw = sb("w3_raw", [P, 2, QK, D // 2], F32, early)
        w2_raw = sb("w2_raw", [P, G, K, GW], F32, early)
        qrow = sb("qrow", [NB, D], F32, early)
        zeros = sb("zeros", [P, T], mybir.dt.bfloat16, early)
        early.close()
        wb_hi = sb("wb_hi", [P, NCH * CW], F32R)
        wb_lo = sb("wb_lo", [P, NCH * CW], F32R)

        phase1 = ExitStack()
        w2_hi = sb("w2_hi", [P, G, K, GW], F32R, phase1)
        w2_lo = sb("w2_lo", [P, G, K, GW], F32R, phase1)
        phase1.close()
        res = sb("res", [P, K, T])
        a_sb = sb("a_sb", [AC, T])
        hw = sb("hw", [AC, T])
        hw_hi = sb("hw_hi", [AC, T], F32R)
        hw_lo = sb("hw_lo", [AC, T], F32R)
        wtok = sb("wtok", [P, TT, E])
        logits = sb("logits", [P, TT, E])
        lmax = sb("lmax", [P, TT])
        shifted = sb("shifted", [P, TT, E])
        ex = sb("ex", [P, TT, E])
        den = sb("den", [P, TT])
        rden = sb("rden", [P, TT])
        gates = sb("gates", [P, TT, E])
        beats = sb("beats", [P, TT, E, E])
        ties = sb("ties", [P, TT, E, E])
        rank = sb("rank", [P, TT, E])

        wbv_hi = wb_hi[:, :].rearrange("p (k n) -> p k n", k=K)
        wbv_lo = wb_lo[:, :].rearrange("p (k n) -> p k n", k=K)

        ps = ctx.enter_context(nc.psum_tensor("ps", [P, 8, T], F32))
        A_BANK, GATE_BANK = 6, 7
        Q_BANK, QT_BANK = 4, 6
        q_tok = [ps[:, QT_BANK + h, 0:HALF * NB].rearrange("p (m b) -> p m b", b=NB) for h in range(2)]
        tok = ps[:, GATE_BANK, 0:TT * E].rearrange("p (t c) -> p t c", t=TT)

        warm_set = sem("warm_set")
        cond_loaded = sem("cond_loaded")
        bias_loaded = sem("bias_loaded")
        w3_loaded = [sem(f"w3_loaded{n}") for n in range(2 * QK)]
        w2_loaded = [sem(f"w2_loaded{n}") for n in range(FIRST + 2 * (G - 1))]
        q_sum = sem("q_sum")
        q_copied = sem("q_copied")
        q_turned = sem("q_turned")
        q_biased = sem("q_biased")
        q_ready = sem("q_ready")
        w2_hi_done = sem("w2_hi_done")
        w2_lo_done = sem("w2_lo_done")
        const_step = sem("const_step")
        wrow_set = sem("wrow_set")
        w_loaded = sem("w_loaded")
        w_hi_done = sem("w_hi_done")
        w_split = sem("w_split")
        tile_loaded = [sem(f"tile_loaded{k}") for k in range(K)]
        sum_done = sem("sum_done")
        act_sum_done = sem("act_sum_done")
        mean_done = sem("mean_done")
        x1_ready = sem("x1_ready")
        hi_done = sem("hi_done")
        lo_done = sem("lo_done")
        x1_used = sem("x1_used")
        y_used = sem("y_used")
        y_psum = sem("y_psum")
        y_evac = sem("y_evac")
        y_stored = [sem(f"y_stored{r}") for r in range(YS)]
        a_psum = sem("a_psum")
        a_copied = sem("a_copied")
        tok_ready = sem("tok_ready")
        gate_step = sem("gate_step")
        shift_ready = sem("shift_ready")
        exp_done = sem("exp_done")
        wrow_ready = sem("wrow_ready")
        wT_ready = sem("wT_ready")
        hw_ready = sem("hw_ready")
        hw_hi_done = sem("hw_hi_done")
        hw_lo_done = sem("hw_lo_done")
        out_psum = sem("out_psum")
        out_evac = sem("out_evac")
        res_loaded = [sem(f"res_loaded{m}") for m in range(K)]
        out_stored = [sem(f"out_stored{m}") for m in range(K)]

        W2_PIECES = ([(0, slice(n * FK, (n + 1) * FK)) for n in range(FIRST)]
                     + [(g, slice(h * HALF, (h + 1) * HALF)) for g in range(1, G) for h in range(2)])
        W2_PIECE_OF = {(g, k): n for n, (g, ks) in enumerate(W2_PIECES) for k in range(K)[ks]}
        ON_DVE = range(0, 2)
        ON_ACT = range(2, K)

        PAIR_OF = [0, 1, 2, 1]
        DONE_ORDER = [1, 0, 2, 3]
        out_order = [PAIR * g + j for g in DONE_ORDER for j in range(PAIR)]
        pos = {m: n for n, m in enumerate(out_order)}
        LATE = out_order[-PAIR:]

        block = ctx.enter_context(nc.Block())

        @block.sync
        def _(sp):
            def load_x(i, k):
                sp.dma_start(stage[:, k, :], xT[i, k]).then_inc(tile_loaded[k], 16)

            def next_x(i):
                for k in range(K):
                    sp.wait_ge(lo_done, K * (i - 1) + k + 1)
                    load_x(i, k)

            def load_y(i):
                for k in range(K):
                    sp.wait_ge(lo_done, K * (NB + i - 1) + k + 1)
                    sp.wait_ge(y_stored[k % YS], 16 * ((K // YS) * i + k // YS + 1))
                    sp.dma_start(stage[:, k, :], y_dram[i, k]).then_inc(tile_loaded[k], 16)

            def wbase_piece(c):
                sp.wait_ge(w_split, EARLY_W + c)
                sp.dma_start(wstage[:, 0:CW], wbase[c]).then_inc(w_loaded, 16)

            def store_y(i):
                for m in range(K):
                    sp.wait_ge(y_evac, K * i + m + 1)
                    sp.dma_start(y_dram[i, m], yring[:, m % YS, :]).then_inc(y_stored[m % YS], 16)

            sp.dma_start(cond_sb[:], condT).then_inc(cond_loaded, 16)
            sp.dma_start(b3_sb[:], b3).then_inc(bias_loaded, 16)
            def load_w3(h):
                for k in range(QK):
                    sp.dma_start(w3_raw[:, h, k], w3[h, k]).then_inc(w3_loaded[h * QK + k], 16)

            def load_w2(n):
                g, ks = W2_PIECES[n]
                sp.dma_start(w2_raw[:, g, ks, :], w2[g, :, ks, :]).then_inc(w2_loaded[n], 16)

            load_w3(0)
            load_x(0, 0)
            load_w2(0)
            load_x(0, 1)
            load_w3(1)
            for k in range(2, K):
                load_x(0, k)
                if k % FK == FK - 1:
                    load_w2(k // FK)
            for n in range(FIRST, len(W2_PIECES)):
                load_w2(n)
            sp.dma_start(b2_sb[:], b2).then_inc(bias_loaded, 16)
            sp.dma_start(bb_sb[:], bbase).then_inc(bias_loaded, 16)
            sp.dma_start(br_sb[:], brouter.partition_broadcast(P)).then_inc(bias_loaded, 16)
            sp.dma_start(wstage[:, 0:K * AC], acat).then_inc(w_loaded, 16)
            next_x(1)
            sp.wait_ge(w_split, 1)
            sp.dma_start(wstage[0:AC, :], bcat).then_inc(w_loaded, 16)
            store_y(0)
            wbase_piece(0)
            with sp.Fori(1, NB - 1) as i:
                next_x(i + 1)
                wbase_piece(i)
                store_y(i)
            load_y(0)
            wbase_piece(NB - 1)
            store_y(NB - 1)

            def load_res(i, tiles, first):
                for m in tiles[0::PAIR]:
                    if not first:
                        for j in range(PAIR):
                            sp.wait_ge(out_stored[m + j], 16 * i)
                    for j in reversed(range(PAIR)):
                        sp.dma_start(res[:, m + j, :], xT[i, m + j]).then_inc(res_loaded[m + j], 16)

            def store_out(i, tiles):
                for m in tiles:
                    sp.wait_ge(out_evac, K * i + pos[m] + 1)
                    sp.dma_start(outT[i, m], res[:, m, :]).then_inc(out_stored[m], 16)

            sp.wait_ge(y_psum, K * NB)
            load_res(0, out_order, True)
            load_y(1)
            store_out(0, out_order[:-PAIR])
            with sp.Fori(1, NB - 1) as i:
                store_out(i - 1, LATE)
                load_res(i, out_order[:-PAIR], False)
                load_y(i + 1)
                load_res(i, LATE, False)
                store_out(i, out_order[:-PAIR])
            store_out(NB - 2, LATE)
            load_res(NB - 1, out_order, False)
            store_out(NB - 1, out_order)
            for m in range(K):
                sp.wait_ge(out_stored[m], 16 * NB)

        @block.gpsimd
        def _(pool):
            nc.gpsimd.memset(ident[:], 0.0).then_inc(const_step, 1)
            nc.gpsimd.memset(earlier[:], 0.0).then_inc(const_step, 1)
            nc.gpsimd.memset(wrow[:, :, 0:E], 0.0).then_inc(wrow_set, 1)
            nc.gpsimd.memset(wrow[:, :, E:AC], 1.0).then_inc(wrow_set, 1)
            pool.wait_ge(const_step, 2)
            nc.gpsimd.affine_select(out=ident[:], in_=ident[:], compare_op=ALU.not_equal, fill=1.0, base=0,
                                    pattern=[[-1, P]], channel_multiplier=1).then_inc(const_step, 1)
            for e in range(1, E):
                nc.gpsimd.memset(earlier[:, e, 0:e], 1.0).then_inc(const_step, 1)

            for n, (g, ks) in enumerate(W2_PIECES):
                pool.wait_ge(w2_hi_done, n + 1)
                nc.gpsimd.tensor_tensor(w2_lo[:, g, ks, :], w2_raw[:, g, ks, :], w2_hi[:, g, ks, :].bitcast(F32),
                                        ALU.subtract).then_inc(w2_lo_done, 1)

            def split(n, raw, hi, lo):
                pool.wait_ge(w_loaded, 16 * (n + 1))
                nc.gpsimd.tensor_copy(hi, raw).then_inc(w_hi_done, 1)
                pool.wait_ge(w_hi_done, n + 1)
                nc.gpsimd.tensor_tensor(lo, raw, hi.bitcast(F32), ALU.subtract).then_inc(w_split, 1)

            split(0, wstage[:, 0:K * AC], a_hi[:, :, :].rearrange("p k n -> p (k n)"),
                  a_lo[:, :, :].rearrange("p k n -> p (k n)"))
            split(1, wstage[0:AC, :], low_hi[:, :], low_lo[:, :])
            pool.wait_ge(q_turned, 2)
            pool.wait_ge(w2_lo_done, len(W2_PIECES))
            with pool.Fori(0, NCH) as c:
                cols = bass.ds(c * CW, CW)
                split(EARLY_W + c, wstage[:, 0:CW], wb_hi[:, cols], wb_lo[:, cols])

        @block.scalar
        def _(act):
            def split_w2_hi(n):
                g, ks = W2_PIECES[n]
                act.wait_ge(w2_loaded[n], 16)
                nc.scalar.activation(w2_hi[:, g, ks, :], w2_raw[:, g, ks, :], ACT.Copy).then_inc(w2_hi_done, 1)

            def sum_x(k):
                act.wait_ge(tile_loaded[k], 16)
                nc.scalar.activation(stage[:, k, :], stage[:, k, :], ACT.Copy,
                                     accum_out=vsum[:, k:k + 1]).then_inc(act_sum_done, 1)

            def x1_free(i, k):
                if k < K - 1:
                    act.wait_ge(x1_used, (K - 1) * i + k + 1)
                else:
                    act.wait_ge(y_psum, K * (i + 1))

            def x_hi(i, k, first=False):
                act.wait_ge(x1_ready, K * i + k + 1)
                if not first:
                    x1_free(i - 1, k)
                nc.scalar.activation(act_hi[:, k, :], stage[:, k, :], ACT.Copy).then_inc(hi_done, 1)

            def y_hi(i, first=False):
                for k in range(K):
                    act.wait_ge(tile_loaded[k], 16 * (NB + i + 1))
                    if first:
                        x1_free(NB - 1, k)
                    else:
                        act.wait_ge(y_used, K * (i - 1) + k + 1)
                    nc.scalar.activation(act_hi[:, k, :], stage[:, k, :], ACT.Copy).then_inc(hi_done, 1)

            def evac_y(i, tiles, first):
                for m in tiles:
                    act.wait_ge(y_psum, K * i + m + 1)
                    if m >= YS or not first:
                        act.wait_ge(y_stored[m % YS], 16 * ((K // YS) * i + m // YS))
                    nc.scalar.activation(yring[:, m % YS, :], ps[:, m % (2 * PAIR), :], ACT.Relu,
                                         bias=b2_sb[:, m:m + 1]).then_inc(y_evac, 1)

            SOON = range(K - PAIR)
            LAST = range(K - PAIR, K)

            split_w2_hi(0)
            x_hi(0, 0, True)
            x_hi(0, 1, True)
            for k in range(2, K):
                sum_x(k)
                if k % FK == 0:
                    split_w2_hi(k // FK)
                if k > 2:
                    x_hi(0, k - 1, True)
            split_w2_hi(FIRST)
            x_hi(0, K - 1, True)
            for n in range(FIRST + 1, len(W2_PIECES)):
                split_w2_hi(n)
            act.wait_ge(bias_loaded, 16 * 4)
            evac_y(0, SOON, True)
            for k in range(K):
                x_hi(1, k)
            evac_y(0, LAST, True)
            with act.Fori(1, NB - 1) as i:
                evac_y(i, SOON, False)
                for k in range(K):
                    x_hi(i + 1, k)
                evac_y(i, LAST, False)
            evac_y(NB - 1, SOON, False)
            y_hi(0, True)
            evac_y(NB - 1, LAST, False)

            def gate(i):
                act.wait_ge(a_psum, i + 1)
                nc.scalar.activation(a_sb[:], ps[0:AC, A_BANK, :], ACT.Copy).then_inc(a_copied, 1)
                act.wait_ge(shift_ready, i + 1)
                nc.scalar.activation(ex[:], shifted[:], ACT.Exp).then_inc(exp_done, 1)
                act.wait_ge(hw_ready, i + 1)
                nc.scalar.activation(hw_hi[:], hw[:], ACT.Copy).then_inc(hw_hi_done, 1)

            with act.Fori(0, NB - 1) as i:
                gate(i)
                y_hi(i + 1)
            gate(NB - 1)

        @block.vector
        def _(dve):
            def condition(h):
                part = qn[:, h * HALF:(h + 1) * HALF, :]
                bias = b3_sb[:, h * HALF:(h + 1) * HALF].unsqueeze(2).to_broadcast([P, HALF, NB])
                dve.wait_ge(q_turned, h + 1)
                nc.vector.tensor_tensor(part, q_tok[h], bias, ALU.add).then_inc(q_biased, 1)
                dve.wait_ge(q_biased, h + 1)
                nc.vector.tensor_scalar(part, part, 0.0, float(T), ALU.max, ALU.mult).then_inc(q_ready, 1)

            def copy_q(h):
                dve.wait_ge(q_sum, h + 1)
                nc.vector.tensor_copy(qrow[:, h * (D // 2):(h + 1) * (D // 2)],
                                      ps[0:NB, Q_BANK + h, :]).then_inc(q_copied, 1)

            def sum_x(i, k):
                dve.wait_ge(tile_loaded[k], 16 * (i + 1))
                nc.vector.reduce_sum(vsum[:, k:k + 1], stage[:, k, :], axis=AX.X).then_inc(sum_done, 1)

            def mean_x(k, summed, n):
                dve.wait_ge(summed, n)
                nc.vector.tensor_scalar(vmean[:, k:k + 1], vsum[:, k:k + 1], 1.0 / T, None,
                                        ALU.mult).then_inc(mean_done, 1)

            def scale_x(i, k):
                dve.wait_ge(mean_done, K * i + k + 1)
                nc.vector.tensor_scalar(stage[:, k, :], stage[:, k, :], vmean[:, k:k + 1],
                                        qn[:, k, bass.ds(i, 1)], ALU.add, ALU.mult).then_inc(x1_ready, 1)

            def act_low(i, k):
                dve.wait_ge(hi_done, K * i + k + 1)
                nc.vector.tensor_tensor(act_lo[:, k, :], stage[:, k, :], act_hi[:, k, :].bitcast(F32),
                                        ALU.subtract).then_inc(lo_done, 1)

            nc.vector.memset(zeros[:], 0.0).then_inc(warm_set, 1)
            dve.wait_ge(bias_loaded, 16)
            def first_mean(k):
                if k in ON_ACT:
                    mean_x(k, act_sum_done, ON_ACT.index(k) + 1)
                else:
                    mean_x(k, sum_done, ON_DVE.index(k) + 1)

            sum_x(0, 0)
            copy_q(0)
            sum_x(0, 1)
            first_mean(0)
            first_mean(1)
            condition(0)
            dve.wait_ge(q_ready, 1)
            scale_x(0, 0)
            scale_x(0, 1)
            act_low(0, 0)
            copy_q(1)
            for k in range(2, K):
                if k == HALF:
                    condition(1)
                    dve.wait_ge(q_ready, 2)
                first_mean(k)
                scale_x(0, k)
                act_low(0, k - 1)
            act_low(0, K - 1)
            with dve.Fori(1, NB) as i:
                for k in range(K):
                    sum_x(i, k)
                    mean_x(k, sum_done, K * i + k + 1 - len(ON_ACT))
                    scale_x(i, k)
                for k in range(K):
                    act_low(i, k)

            def evac_out(i, tiles):
                for m in tiles:
                    dve.wait_ge(out_psum, K * i + pos[m] + 1)
                    dve.wait_ge(res_loaded[m], 16 * (i + 1))
                    bank = PAIR * PAIR_OF[m // PAIR] + m % PAIR
                    nc.vector.scalar_tensor_tensor(res[:, m, :], ps[:, bank, :], bb_sb[:, m:m + 1], res[:, m, :],
                                                   ALU.add, ALU.add).then_inc(out_evac, 1)

            STEPS = 11

            def gate(i):
                step = [0]

                def then_next(ins):
                    step[0] += 1
                    ins.then_inc(gate_step, 1)
                    dve.wait_ge(gate_step, STEPS * i + step[0])

                over_experts = [P, TT, E]
                dve.wait_ge(tok_ready, i + 1)
                then_next(nc.vector.tensor_tensor(logits[:], tok,
                                                  br_sb[:, :].unsqueeze(1).to_broadcast(over_experts), ALU.add))
                then_next(nc.vector.reduce_max(lmax[:], logits[:], axis=AX.X))
                nc.vector.tensor_tensor(shifted[:], logits[:], lmax[:, :].unsqueeze(2).to_broadcast(over_experts),
                                        ALU.subtract).then_inc(shift_ready, 1)
                dve.wait_ge(exp_done, i + 1)
                then_next(nc.vector.reduce_sum(den[:], ex[:], axis=AX.X))
                then_next(nc.vector.reciprocal(rden[:], den[:]))
                then_next(nc.vector.tensor_tensor(gates[:], ex[:], rden[:, :].unsqueeze(2).to_broadcast(over_experts),
                                                  ALU.mult))
                pairs = [P, TT, E, E]
                other = gates[:, :, :].unsqueeze(2).to_broadcast(pairs)
                own = gates[:, :, :].unsqueeze(3).to_broadcast(pairs)
                then_next(nc.vector.tensor_tensor(beats[:], other, own, ALU.is_gt))
                then_next(nc.vector.tensor_tensor(ties[:], other, own, ALU.is_equal))
                then_next(nc.vector.tensor_tensor(
                    ties[:], ties[:], earlier[:, :, :].unsqueeze(1).to_broadcast(pairs), ALU.mult))
                then_next(nc.vector.tensor_tensor(beats[:], beats[:], ties[:], ALU.add))
                then_next(nc.vector.reduce_sum(rank[:], beats[:], axis=AX.X))
                then_next(nc.vector.scalar_tensor_tensor(wtok[:], rank[:], 1.5, gates[:], ALU.is_lt, ALU.mult))
                assert step[0] == STEPS
                nc.vector.tensor_copy(wrow[:, :, E:E + E * R].rearrange("p t (e r) -> p t e r", r=R),
                                      wtok[:, :, :].unsqueeze(3).to_broadcast([P, TT, E, R])).then_inc(wrow_ready, 1)
                dve.wait_ge(wT_ready, i + 1)
                nc.vector.tensor_tensor(hw[:], a_sb[:], ps[0:AC, GATE_BANK, :], ALU.mult).then_inc(hw_ready, 1)
                dve.wait_ge(hw_hi_done, i + 1)
                nc.vector.tensor_tensor(hw_lo[:], hw[:], hw_hi[:, :].bitcast(F32),
                                        ALU.subtract).then_inc(hw_lo_done, 1)

            dve.wait_ge(bias_loaded, 16 * 4)
            dve.wait_ge(const_step, 2 + E)
            dve.wait_ge(wrow_set, 2)
            for k in range(K):
                act_low(NB, k)
            with dve.Fori(0, NB - 1) as i:
                gate(i)
                evac_out(i, out_order[:-PAIR])
                for k in range(K):
                    act_low(NB + i + 1, k)
                evac_out(i, LATE)
            gate(NB - 1)
            evac_out(NB - 1, out_order)

        @block.tensor
        def _(pe):
            def three(out, w_hi, w_lo, a_h, a_l, start, stop):
                nc.tensor.matmul(out, w_hi, a_h, start=start, stop=False)
                nc.tensor.matmul(out, w_hi, a_l, start=False, stop=False)
                return nc.tensor.matmul(out, w_lo, a_h, start=False, stop=stop)

            def project(h, ks):
                for k in ks:
                    pe.wait_ge(w3_loaded[h * QK + k], 16)
                    mm = nc.tensor.matmul(ps[0:NB, Q_BANK + h, :], cond_sb[:, k, :], w3_raw[:, h, k, :],
                                          start=(k == 0), stop=(k == QK - 1))
                if k == QK - 1:
                    mm.then_inc(q_sum, 1)

            def turn(h):
                pe.wait_ge(q_copied, h + 1)
                for m in range(HALF):
                    cols = slice((h * HALF + m) * P, (h * HALF + m + 1) * P)
                    tr = nc.tensor.transpose(q_tok[h][:, m, :], qrow[:, cols], ident[0:NB, 0:NB])
                tr.then_inc(q_turned, 1)

            pe.wait_ge(warm_set, 1)
            for _ in range(WARM):
                nc.tensor.matmul(ps[:, GATE_BANK, :], zeros[:, 0:P], zeros[:], start=True, stop=True)
            pe.wait_ge(cond_loaded, 16)
            project(0, range(QK))
            project(1, range(1))
            pe.wait_ge(const_step, 3)
            turn(0)
            project(1, range(1, QK))

            def y_group(i, g, first):
                bank = PAIR * (g % 2)
                if g >= 2 or not first:
                    pe.wait_ge(y_evac, K * i + PAIR * (g - 1))
                for k in range(K):
                    if first:
                        pe.wait_ge(w2_lo_done, W2_PIECE_OF[g, k] + 1)
                    if first and g == 0 and k == 1:
                        turn(1)
                    if g == 0:
                        pe.wait_ge(lo_done, K * i + k + 1)
                    for j in range(PAIR):
                        cols = slice(j * P, (j + 1) * P)
                        mm = three(ps[:, bank + j, :], w2_hi[:, g, k, cols], w2_lo[:, g, k, cols],
                                   act_hi[:, k, :], act_lo[:, k, :], k == 0, k == K - 1)
                        if k == K - 1:
                            mm.then_inc(y_psum, 1)
                        elif g == G - 1 and j == PAIR - 1:
                            mm.then_inc(x1_used, 1)

            for g in range(G):
                y_group(0, g, True)
            with pe.Fori(1, NB) as i:
                for g in range(G):
                    y_group(i, g, False)

            def base_tiles(i, g, k):
                for j in range(PAIR):
                    cols = slice((PAIR * g + j) * P, (PAIR * g + j + 1) * P)
                    mm = three(ps[:, PAIR * PAIR_OF[g] + j, :], wbv_hi[:, k, cols], wbv_lo[:, k, cols],
                               act_hi[:, k, :], act_lo[:, k, :], k == 0, False)
                return mm

            def low_rank(i, g):
                for j in range(PAIR):
                    cols = slice((PAIR * g + j) * P, (PAIR * g + j + 1) * P)
                    three(ps[:, PAIR * PAIR_OF[g] + j, :], low_hi[:, cols], low_lo[:, cols],
                          hw_hi[:, :], hw_lo[:, :], False, True).then_inc(out_psum, 1)

            def batch(i, first):
                for k in range(K):
                    pe.wait_ge(lo_done, K * (NB + i) + k + 1)
                    base_tiles(i, 0, k)
                    mm = three(ps[0:AC, A_BANK, :], a_hi[:, k, :], a_lo[:, k, :], act_hi[:, k, :], act_lo[:, k, :],
                               k == 0, k == K - 1)
                mm.then_inc(a_psum, 1)
                if first:
                    pe.wait_ge(y_evac, K * NB)
                else:
                    pe.wait_ge(out_evac, K * i)
                for k in range(K):
                    if k == HALF:
                        pe.wait_ge(a_copied, i + 1)
                    base_tiles(i, 1, k)
                    if k == HALF:
                        for t in range(TT):
                            tr = nc.tensor.transpose(tok[:, t, :], a_sb[0:E, t * P:(t + 1) * P], ident[0:E, 0:E])
                        tr.then_inc(tok_ready, 1)
                for k in range(K):
                    if k == HALF:
                        pe.wait_ge(wrow_ready, i + 1)
                        for t in range(TT):
                            tr = nc.tensor.transpose(ps[0:AC, GATE_BANK, t * P:(t + 1) * P], wrow[:, t, :], ident[:])
                        tr.then_inc(wT_ready, 1)
                    base_tiles(i, 2, k)
                pe.wait_ge(hw_lo_done, i + 1)
                for g in DONE_ORDER[:-1]:
                    low_rank(i, g)
                pe.wait_ge(out_evac, K * i + PAIR)
                for k in range(K):
                    base_tiles(i, 3, k).then_inc(y_used, 1)
                low_rank(i, 3)

            pe.wait_ge(y_evac, K * NB - PAIR)
            pe.wait_ge(w_split, EARLY_W + NCH)
            batch(0, True)
            with pe.Fori(1, NB) as i:
                batch(i, False)


def kernel(x, cond_1024, L0_cond_W3, L0_cond_b3, L0_cond_W2, L0_cond_b2, L0_ffn_W_base, L0_ffn_b_base, L0_ffn_A_s,
           L0_ffn_B_s, L0_ffn_A_r, L0_ffn_B_r, L0_ffn_W_router, L0_ffn_b_router):
    import numpy as np
    import concourse.bacc as bacc
    from concourse import mybir as mb
    from concourse.bass_utils import run_bass_kernel_spmd as run

    x, cond, w3, b3, w2, b2, wbase, bbase, a_s, b_s, a_r, b_r, w_router, b_router = (
        np.asarray(a) for a in (x, cond_1024, L0_cond_W3, L0_cond_b3, L0_cond_W2, L0_cond_b2, L0_ffn_W_base,
                                L0_ffn_b_base, L0_ffn_A_s, L0_ffn_B_s, L0_ffn_A_r, L0_ffn_B_r, L0_ffn_W_router,
                                L0_ffn_b_router))
    nb, t, d = x.shape
    e, _, r = a_r.shape
    k = d // P
    q = cond.shape[1]
    g = k // PAIR
    columns = lambda v: v.reshape(k, P).T
    a_all = np.concatenate([w_router, a_r.transpose(1, 0, 2).reshape(d, e * r), a_s], axis=1)
    arrays = {
        "xT": x.transpose(0, 2, 1).reshape(nb, k, P, t),
        "condT": cond.T.reshape(q // P, P, nb).transpose(1, 0, 2),
        "w3": w3.reshape(q // P, P, 2, d // 2).transpose(2, 0, 1, 3),
        "b3": columns(b3),
        "w2": w2.reshape(k, P, g, PAIR * P).transpose(2, 1, 0, 3),
        "b2": columns(b2),
        "wbase": wbase.reshape(k, P, 2, d // 2).transpose(0, 2, 1, 3).reshape(2 * k, P, d // 2),
        "bbase": columns(bbase),
        "acat": a_all.reshape(k, P, -1).transpose(1, 0, 2).reshape(P, -1),
        "bcat": np.concatenate([np.zeros((e, d), b_r.dtype), b_r.reshape(e * r, d), b_s], axis=0),
        "brouter": b_router,
    }
    arrays = {f"in_{n}": np.ascontiguousarray(a) for n, a in arrays.items()}
    nc = bacc.Bacc("TRN2", target_bir_lowering=False, num_devices=1)
    args = [nc.dram_tensor(n, a.shape, mb.dt.from_np(a.dtype), kind="ExternalInput").ap() for n, a in arrays.items()]
    out = nc.dram_tensor("outT", (nb, k, P, t), mb.dt.from_np(x.dtype), kind="ExternalOutput").ap()
    adaln_ffn(nc, *args, out, e, r)
    got = run(nc, [arrays], core_ids=[0]).results[0]["outT"]
    return np.ascontiguousarray(got.reshape(nb, d, t).transpose(0, 2, 1))
```
